# Optimizing a Trainium2 kernel written in Bass

```python
import numpy as np
import jax
import jax.numpy as jnp

def _softmax(x, axis=-1):
    return jax.nn.softmax(x, axis=axis)

def _gelu(x):
    return jax.nn.gelu(x, approximate=True)

def _silu(x):
    return jax.nn.silu(x)

def _sigmoid(x):
    return jax.nn.sigmoid(x)

def _layernorm(x, axis=-1, eps=1e-05):
    m = jnp.mean(x, axis=axis, keepdims=True)
    v = jnp.var(x, axis=axis, keepdims=True)
    return (x - m) / jnp.sqrt(v + eps)

def _scatter_add(tgt, idx, src, axis=0):
    return tgt.at[idx].add(src)

def _segment_sum(src, seg, n):
    return jax.ops.segment_sum(src, seg, n)
kernel_name = 'mk_cond_resid_d2_seqx_r4_9ea1a3'

def setup_inputs(seed: int=0):
    np.random.seed(seed)
    _w = jnp.asarray

    def _rec_inputs():
        import jax
        import jax.numpy as jnp
        _rk = jax.random.key(seed)
        x = -7.109e-05 + 0.9999 * jax.random.normal(jax.random.fold_in(_rk, 1), (8, 256, 1024), jnp.float32)
        _lenS = 256 - jax.random.randint(jax.random.fold_in(_rk, 7), (8,), 0, max(1, 256 // 4) + 1, jnp.int32)
        _lenS2 = 256 - jax.random.randint(jax.random.fold_in(_rk, 8), (8,), 0, max(1, 256 // 4) + 1, jnp.int32)
        itok_B_1_14 = jax.random.randint(jax.random.fold_in(_rk, 11), (8,), 1, 15, jnp.int32)
        itok_B_0_7 = jax.random.randint(jax.random.fold_in(_rk, 12), (8,), 0, 8, jnp.int32)
        return (x, itok_B_1_14, itok_B_0_7)
    x, itok_B_1_14, itok_B_0_7 = _rec_inputs()

    def _L0_cond_setup():
        import jax, jax.numpy as jnp
        import numpy as np
        B, S, D_IN = (8, 512, 1024)
        A, D_OUT = (16, 1024)
        key = jax.random.key(seed)
        k1, k2, k3 = jax.random.split(key, 3)
        x = jax.random.normal(k1, (B, S, D_IN), dtype=jnp.float32)
        weight = jax.random.normal(k2, (A, D_OUT, D_IN), dtype=jnp.float32) * 0.02
        adapter_ids = jax.random.randint(k3, (B,), 0, A, dtype=jnp.int64)
        return {'x': x, 'weight': weight, 'adapter_ids': adapter_ids}
    _L0_cond_all = _L0_cond_setup()
    _L0_cond_in = {k: v for k, v in _L0_cond_all.items() if k in ('weight',)}
    del _L0_cond_all

    def _L1_cond_setup():
        import jax, jax.numpy as jnp
        import numpy as np
        TOP_K = 2
        LANG_BIAS = 5.0
        SCALING = 32.0 / 16.0
        LANGUAGE_PAD_ID = -1
        key = jax.random.key(seed)
        ks = jax.random.split(key, 6)
        B, T, D, O, E, R = (4, 512, 1024, 1024, 8, 16)
        x = jax.random.normal(ks[0], (B, T, D), dtype=jnp.float32)
        language_ids = jax.random.randint(ks[1], (B,), 0, E).astype(jnp.int64)
        W = jax.random.normal(ks[2], (O, D), dtype=jnp.float32) * (1.0 / np.sqrt(D))
        Wr = jax.random.normal(ks[3], (E, D), dtype=jnp.float32) * (1.0 / np.sqrt(D))
        A = jax.random.normal(ks[4], (E, R, D), dtype=jnp.float32) * (1.0 / np.sqrt(D))
        Bm = jax.random.normal(ks[5], (O, R), dtype=jnp.float32) * 0.0
        Bm = jnp.broadcast_to(Bm, (E, O, R)) + jax.random.normal(ks[5], (E, O, R), dtype=jnp.float32) * 0.02
        return {'x': x, 'language_ids': language_ids, 'W': W, 'Wr': Wr, 'A': A, 'B': Bm}
    _L1_cond_all = _L1_cond_setup()
    _L1_cond_in = {k: v for k, v in _L1_cond_all.items() if k in ('W', 'Wr', 'A', 'B')}
    del _L1_cond_all
    return {'x': x, 'itok_B_1_14': itok_B_1_14, 'itok_B_0_7': itok_B_0_7, 'L0_cond_weight': _L0_cond_in['weight'], 'L1_cond_W': _L1_cond_in['W'], 'L1_cond_Wr': _L1_cond_in['Wr'], 'L1_cond_A': _L1_cond_in['A'], 'L1_cond_B': _L1_cond_in['B']}

def reference(x, itok_B_1_14, itok_B_0_7, L0_cond_weight, L1_cond_W, L1_cond_Wr, L1_cond_A, L1_cond_B):
    import jax
    import jax.numpy as jnp

    def _L0_cond_ref(x, weight, adapter_ids):
        import jax, jax.numpy as jnp
        import numpy as np
        B, S, D_IN = (8, 512, 1024)
        A, D_OUT = (16, 1024)
        w = weight[adapter_ids]
        return jnp.einsum('bij,bkj->bik', x, w)

    def _L1_cond_ref(x, language_ids, W, Wr, A, B):
        import jax, jax.numpy as jnp
        import numpy as np
        TOP_K = 2
        LANG_BIAS = 5.0
        SCALING = 32.0 / 16.0
        LANGUAGE_PAD_ID = -1
        base = jnp.einsum('btd,od->bto', x, W)
        E = Wr.shape[0]
        logits = jnp.einsum('btd,ed->bte', x.astype(jnp.float32), Wr.astype(jnp.float32))
        expert_targets = language_ids
        valid = expert_targets >= 0
        tgt = jnp.where(valid, expert_targets, 0)
        bias = jax.nn.one_hot(tgt, E, dtype=logits.dtype) * LANG_BIAS
        bias = jnp.where(valid[:, None], bias, 0.0)
        logits = logits + bias[:, None, :]
        topw, topi = jax.lax.top_k(logits, TOP_K)
        weights = jax.nn.softmax(topw, axis=-1)
        gates = jnp.sum(jax.nn.one_hot(topi, E, dtype=weights.dtype) * weights[..., None], axis=-2)
        gates = gates.astype(x.dtype)
        h = jnp.einsum('btd,erd->bter', x, A)
        lora_out = jnp.einsum('bter,bte,eor->bto', h, gates, B)
        return base + SCALING * lora_out
    x = x + _L0_cond_ref(x, L0_cond_weight, itok_B_1_14)
    x = x + _L1_cond_ref(x, itok_B_0_7, L1_cond_W, L1_cond_Wr, L1_cond_A, L1_cond_B)
    return x

_drawn_inputs = setup_inputs


def setup_inputs(seed=0):
    import zlib

    import numpy as np

    out = dict(_drawn_inputs(seed))
    spreads = {}
    factors = {'L1_cond_Wr': 2.95}
    for name, (base, spread) in spreads.items():
        noise = np.random.default_rng([zlib.crc32(name.encode()), seed]).standard_normal(out[name].shape)
        drawn = base * np.exp(spread * noise) if base else spread * noise
        out[name] = jnp.asarray(drawn.astype(out[name].dtype))
    for name, factor in factors.items():
        out[name] = (out[name] * factor).astype(out[name].dtype)
    return out
```

```python
from contextlib import ExitStack

import concourse.bass as bass
from concourse import mybir

F32 = mybir.dt.float32
F32R = mybir.dt.float32r
I32 = mybir.dt.int32
U32 = mybir.dt.uint32
ALU = mybir.AluOpType
ACT = mybir.ActivationFunctionType

P = 128
NB = 8
TOK = 256
D = 1024
K = D // P
OT = D // P
NE = 8
R = 16
ER = NE * R
NT = TOK // P
LANG_BIAS = 5.0

SEG_AT = [0, 392, 776]
SEG_N = [392, 384, 384]
OUT_AT = [0, 256, 640]
OUT_N = [256, 384, 384]
ROW = sum(SEG_N)
A_AT = 256
R_AT = A_AT + ER

RAW = 4
HL = 4
XP = 4
STEPS = 9


def build(nc, xT, adapter_ids, lang_ids, w_adapt, w_res, b_lora, out):
    with ExitStack() as ctx:
        def sb(name, shape, dt=F32):
            return ctx.enter_context(nc.sbuf_tensor(name, shape, dt))

        def sem(name):
            return ctx.enter_context(nc.semaphore(name))

        w_hl = sb("w_hl", [P, K, 2, ROW], F32R)
        b_hl = sb("b_hl", [P, 2, D], F32R)
        a_raw = sb("a_raw", [P, RAW, K * P])
        a_hl = sb("a_hl", [P, HL, 2, K * P], F32R)
        x_raw = sb("x_raw", [P, K, TOK])
        x_hl = sb("x_hl", [P, K, 2, TOK], F32R)
        y_tmp = sb("y_tmp", [P, 2, TOK])
        y_h = sb("y_h", [P, K, TOK], F32R)
        y_l = sb("y_l", [P, K, TOK], F32R)
        out_sb = sb("out_sb", [P, NT, ROW])
        ident = sb("ident", [P, P])
        iota8 = sb("iota8", [P, NE])
        iota_be = sb("iota_be", [P, NB, NE])
        ids_sb = sb("ids_sb", [1, NB], I32)
        lang_sb = sb("lang_sb", [P, NB], I32)
        bias = sb("bias", [P, NB * NE])
        logits = sb("logits", [P, NE])
        top = sb("top", [P, 8])
        top_at = sb("top_at", [P, 8], U32)
        spare = sb("spare", [P, 1])
        e2 = sb("e2", [P, 1])
        half = sb("half", [P, 1])
        p1 = sb("p1", [P, 1])
        p2 = sb("p2", [P, 1])
        g1 = sb("g1", [P, NE])
        g2 = sb("g2", [P, NE])
        gate = sb("gate", [P, NE])
        hg = sb("hg", [P, ER])
        hgT_h = sb("hgT_h", [P, P], F32R)
        hgT_l = sb("hgT_l", [P, P], F32R)

        acc1 = ctx.enter_context(nc.psum_tensor("acc1", [P, 2, 512], F32))
        acc2 = ctx.enter_context(nc.psum_tensor("acc2", [P, NT, 3, 512], F32))

        ids_in = sem("ids_in")
        lang_in = sem("lang_in")
        x_in = [sem(f"x_in{i}") for i in range(2)]
        a_in = [sem(f"a_in{i}") for i in range(RAW)]
        res_in = [sem(f"res_in{i}") for i in range(2)]
        consts = sem("consts")
        bias_done = sem("bias_done")
        res_diag = sem("res_diag")
        res_high = sem("res_high")
        res_split = sem("res_split")
        x_high = sem("x_high")
        x_split = sem("x_split")
        a_high = sem("a_high")
        a_split = sem("a_split")
        s1_done = sem("s1_done")
        y_part = sem("y_part")
        y_sum = sem("y_sum")
        y_high = sem("y_high")
        y_split = sem("y_split")
        seg0_done = sem("seg0_done")
        step = sem("step")
        exp_done = sem("exp_done")
        hg_done = sem("hg_done")
        hgT_done = sem("hgT_done")
        hgT_high = sem("hgT_high")
        hgT_split = sem("hgT_split")
        lora_done = sem("lora_done")
        evac = [sem(f"evac{t}") for t in range(NT)]
        stored = [sem(f"stored{t}") for t in range(NT)]

        block = ctx.enter_context(nc.Block())

        @block.sync
        def _(sp):
            def load_x(b):
                for i in range(2):
                    ks = slice(i * K // 2, (i + 1) * K // 2)
                    sp.dma_start(x_raw[:, ks, :], xT[b, :, ks, :]).then_inc(x_in[i], 16)

            def load_a(b, a_id, o):
                if not (isinstance(b, int) and o < RAW):
                    sp.wait_ge(a_split, b * OT + o - RAW + 1)
                sp.dma_start(a_raw[:, o % RAW, :], w_adapt[a_id, o]).then_inc(a_in[o % RAW], 16)

            def load_res(j):
                if j >= 2:
                    sp.wait_ge(res_split, j - 1)
                if j < K:
                    sp.dma_start(out_sb[:, j % 2, :], w_res[j]).then_inc(res_in[j % 2], 16)
                else:
                    sp.dma_start(out_sb[:, j % 2, 0:D], b_lora).then_inc(res_in[j % 2], 16)

            def adapter(b):
                return sp.value_load(ids_sb[0:1, bass.ds(b, 1)], min_val=0, max_val=w_adapt.shape[0] - 1)

            sp.dma_start(ids_sb[:], adapter_ids).then_inc(ids_in, 16)
            sp.dma_start(lang_sb[:], lang_ids).then_inc(lang_in, 16)
            load_x(0)
            sp.wait_ge(ids_in, 16)
            a_id = adapter(0)
            for o in range(RAW):
                load_a(0, a_id, o)
            load_res(0)
            load_res(1)
            for o in range(RAW, OT):
                load_a(0, a_id, o)
                load_res(o - 2)
            for j in range(OT - 2, K + 1):
                load_res(j)
            with sp.Fori(1, NB) as b:
                a_id = adapter(b)
                for o in range(RAW):
                    load_a(b, a_id, o)
                sp.wait_ge(y_sum, b * OT)
                load_x(b)
                for o in range(RAW, OT):
                    load_a(b, a_id, o)

        @block.gpsimd
        def _(pool):
            nc.gpsimd.memset(ident[:], 0.0).then_inc(consts, 1)
            pool.wait_ge(consts, 1)
            nc.gpsimd.affine_select(out=ident[:], in_=ident[:], compare_op=ALU.not_equal, fill=1.0, base=0,
                                    pattern=[[-1, P]], channel_multiplier=1).then_inc(consts, 1)
            nc.gpsimd.iota(iota8[:], pattern=[[1, NE]], base=0, channel_multiplier=0,
                           allow_small_or_imprecise_dtypes=True).then_inc(consts, 1)
            nc.gpsimd.iota(iota_be[:], pattern=[[0, NB], [1, NE]], base=0, channel_multiplier=0,
                           allow_small_or_imprecise_dtypes=True).then_inc(consts, 1)
            pool.wait_ge(consts, 4)
            for j in range(K + 1):
                pool.wait_ge(res_in[j % 2], 16 * (j // 2 + 1))
                if j < K:
                    at = j * P if j * P < OUT_N[0] else SEG_AT[1] - OUT_AT[1] + j * P
                    diag = out_sb[:, j % 2, at:at + P]
                    nc.gpsimd.tensor_tensor(diag, diag, ident[:], ALU.add).then_inc(res_diag, 1)
                pool.wait_ge(res_high, j + 1)
                if j < K:
                    high, low, n = w_hl[:, j, 0, :], w_hl[:, j, 1, :], ROW
                else:
                    high, low, n = b_hl[:, 0, :], b_hl[:, 1, :], D
                nc.gpsimd.tensor_tensor(low, out_sb[:, j % 2, 0:n], high.bitcast(F32),
                                        ALU.subtract).then_inc(res_split, 1)

        @block.scalar
        def _(act):
            def high_x(b):
                for i in range(XP):
                    ks = slice(i * K // XP, (i + 1) * K // XP)
                    act.wait_ge(x_in[i * 2 // XP], 16 * b + 16)
                    if i == 0 and not isinstance(b, int):
                        act.wait_ge(s1_done, b * OT)
                    nc.scalar.copy(x_hl[:, ks, 0, :], x_raw[:, ks, :]).then_inc(x_high, 1)

            def high_a(b, o):
                act.wait_ge(a_in[o % RAW], 16 * (b * (OT // RAW) + o // RAW + 1))
                if not (isinstance(b, int) and b == 0 and o < HL):
                    act.wait_ge(s1_done, b * OT + o - HL + 1)
                nc.scalar.copy(a_hl[:, o % HL, 0, :], a_raw[:, o % RAW, :]).then_inc(a_high, 1)

            def high_res(j):
                if j < K:
                    act.wait_ge(res_diag, j + 1)
                    nc.scalar.copy(w_hl[:, j, 0, :], out_sb[:, j % 2, :]).then_inc(res_high, 1)
                else:
                    act.wait_ge(res_in[j % 2], 16 * (j // 2 + 1))
                    nc.scalar.copy(b_hl[:, 0, :], out_sb[:, j % 2, 0:D]).then_inc(res_high, 1)

            def stage1(b, first=False):
                for o in range(OT):
                    if o + HL < OT:
                        high_a(b, o + HL)
                    act.wait_ge(y_sum, b * OT + o + 1)
                    nc.scalar.copy(y_h[:, o, :], y_tmp[:, o % 2, :]).then_inc(y_high, 1)
                    if first:
                        high_res(o)
                if first:
                    high_res(K)

            def ahead(b):
                for o in range(HL):
                    high_a(b, o)
                high_x(b)

            def weight_of_second(b, t):
                act.wait_ge(step, STEPS * (b * NT + t) + 2)
                nc.scalar.activation(e2[:], top[:, 0:1], ACT.Exp, bias=top[:, 1:2],
                                     scale=-1.0).then_inc(exp_done, 1)

            def high_hgT(b, t):
                act.wait_ge(hgT_done, b * NT + t + 1)
                nc.scalar.copy(hgT_h[:], acc1[:, t, 0:P]).then_inc(hgT_high, 1)

            def result(b, t):
                if not (isinstance(b, int) and b == 0):
                    act.wait_ge(stored[t], b * 32)
                for s in range(3):
                    act.wait_ge(lora_done, (b * NT + t) * 3 + s + 1)
                    at = slice(OUT_AT[s], OUT_AT[s] + OUT_N[s])
                    nc.scalar.copy(out_sb[:, t, at], acc2[:, t, s, 0:OUT_N[s]]).then_inc(evac[t], 1)
                    if s > 0:
                        part = slice(0, OUT_AT[2]) if s == 1 else at
                        act.wait_ge(evac[t], b * 3 + s + 1)
                        act.dma_start(out[b, t * P:(t + 1) * P, part], out_sb[:, t, part]).then_inc(stored[t], 16)

            def stage2(b):
                weight_of_second(b, 0)
                high_hgT(b, 0)
                weight_of_second(b, 1)
                high_hgT(b, 1)
                result(b, 0)
                result(b, 1)

            high_x(0)
            for o in range(HL):
                high_a(0, o)
            stage1(0, first=True)
            ahead(1)
            stage2(0)
            with act.Fori(1, NB - 1) as b:
                stage1(b)
                ahead(b + 1)
                stage2(b)
            stage1(NB - 1)
            stage2(NB - 1)
            for t in range(NT):
                act.wait_ge(stored[t], 32 * NB)

        @block.vector
        def _(dve):
            def low_x(b):
                for i in range(XP):
                    ks = slice(i * K // XP, (i + 1) * K // XP)
                    dve.wait_ge(x_high, b * XP + i + 1)
                    nc.vector.tensor_tensor(x_hl[:, ks, 1, :], x_raw[:, ks, :], x_hl[:, ks, 0, :].bitcast(F32),
                                            ALU.subtract).then_inc(x_split, 1)

            def low_a(b, o):
                dve.wait_ge(a_high, b * OT + o + 1)
                nc.vector.tensor_tensor(a_hl[:, o % HL, 1, :], a_raw[:, o % RAW, :],
                                        a_hl[:, o % HL, 0, :].bitcast(F32), ALU.subtract).then_inc(a_split, 1)

            def stage1(b):
                for o in range(OT):
                    y = y_tmp[:, o % 2, :]
                    dve.wait_ge(s1_done, b * OT + o + 1)
                    nc.vector.tensor_tensor(y, acc1[:, o % 2, 0:TOK], x_raw[:, o, :], ALU.add).then_inc(y_part, 1)
                    dve.wait_ge(y_part, b * OT + o + 1)
                    nc.vector.tensor_tensor(y, acc1[:, o % 2, TOK:2 * TOK], y, ALU.add).then_inc(y_sum, 1)
                    if o + HL < OT:
                        low_a(b, o + HL)
                    dve.wait_ge(y_high, b * OT + o + 1)
                    nc.vector.tensor_tensor(y_l[:, o, :], y, y_h[:, o, :].bitcast(F32),
                                            ALU.subtract).then_inc(y_split, 1)

            def ahead(b):
                for o in range(HL):
                    low_a(b, o)
                low_x(b)

            def gates(b, t):
                base = STEPS * (b * NT + t)
                dve.wait_ge(seg0_done, b * NT + t + 1)
                nc.vector.tensor_tensor(logits[:], acc2[:, t, 0, R_AT:R_AT + NE],
                                        bias[:, bass.ds(b * NE, NE)], ALU.add).then_inc(step, 1)
                dve.wait_ge(step, base + 1)
                nc.vector.memset(spare[:], 0.0)
                nc.vector.max(top[:], logits[:]).then_inc(step, 1)
                dve.wait_ge(step, base + 2)
                nc.vector.memset(spare[:], 0.0)
                nc.vector.max_index(top_at[:], top[:], logits[:]).then_inc(step, 1)
                dve.wait_ge(exp_done, b * NT + t + 1)
                nc.vector.tensor_scalar(half[:], e2[:], 1.0, 0.5, ALU.add, ALU.mult).then_inc(step, 1)
                dve.wait_ge(step, base + 4)
                nc.vector.reciprocal(p1[:], half[:]).then_inc(step, 1)
                dve.wait_ge(step, base + 5)
                nc.vector.tensor_tensor(p2[:], p1[:], e2[:], ALU.mult).then_inc(step, 1)
                nc.vector.scalar_tensor_tensor(out=g1[:], in0=iota8[:], scalar=top_at[:, 0:1],
                                               in1=p1[:].to_broadcast([P, NE]), op0=ALU.is_equal,
                                               op1=ALU.mult).then_inc(step, 1)
                dve.wait_ge(step, base + 6)
                nc.vector.scalar_tensor_tensor(out=g2[:], in0=iota8[:], scalar=top_at[:, 1:2],
                                               in1=p2[:].to_broadcast([P, NE]), op0=ALU.is_equal,
                                               op1=ALU.mult).then_inc(step, 1)
                dve.wait_ge(step, base + 8)
                nc.vector.tensor_tensor(gate[:], g1[:], g2[:], ALU.add).then_inc(step, 1)
                dve.wait_ge(step, base + 9)
                nc.vector.tensor_tensor(hg[:].rearrange("p (e r) -> p e r", e=NE),
                                        acc2[:, t, 0, A_AT:A_AT + ER].rearrange("p (e r) -> p e r", e=NE),
                                        gate[:].rearrange("p (e r) -> p e r", r=1).to_broadcast([P, NE, R]),
                                        ALU.mult).then_inc(hg_done, 1)

            def low_hgT(b, t):
                dve.wait_ge(hgT_high, b * NT + t + 1)
                nc.vector.tensor_tensor(hgT_l[:], acc1[:, t, 0:P], hgT_h[:].bitcast(F32),
                                        ALU.subtract).then_inc(hgT_split, 1)

            def stage2(b):
                for t in range(NT):
                    gates(b, t)
                    low_hgT(b, t)

            low_x(0)
            for o in range(HL):
                low_a(0, o)
            dve.wait_ge(consts, 4)
            dve.wait_ge(lang_in, 16)
            nc.vector.tensor_tensor(bias[:].rearrange("p (b e) -> p b e", b=NB), iota_be[:],
                                    lang_sb[:].rearrange("p (b e) -> p b e", e=1).to_broadcast([P, NB, NE]),
                                    ALU.is_equal).then_inc(bias_done, 1)
            dve.wait_ge(bias_done, 1)
            nc.vector.tensor_scalar(bias[:], bias[:], LANG_BIAS, None, ALU.mult).then_inc(bias_done, 1)
            stage1(0)
            ahead(1)
            dve.wait_ge(bias_done, 2)
            stage2(0)
            with dve.Fori(1, NB - 1) as b:
                stage1(b)
                ahead(b + 1)
                stage2(b)
            stage1(NB - 1)
            stage2(NB - 1)

        @block.tensor
        def _(pe):
            def stage1(b):
                for o in range(OT):
                    pe.wait_ge(a_split, b * OT + o + 1)
                    if o >= 2:
                        pe.wait_ge(y_sum, b * OT + o - 1)
                    for k in range(K):
                        if o == 0 and k % (K // XP) == 0:
                            pe.wait_ge(x_split, b * XP + k // (K // XP) + 1)
                        ko = slice(k * P, (k + 1) * P)
                        nc.tensor.matmul(acc1[:, o % 2, :], a_hl[:, o % HL, 0, ko],
                                         x_hl[:, k, :, :].rearrange("p h n -> p (h n)"),
                                         start=(k == 0), stop=False)
                        last = nc.tensor.matmul(acc1[:, o % 2, 0:TOK], a_hl[:, o % HL, 1, ko],
                                                x_hl[:, k, 0, :], start=False, stop=(k == K - 1))
                    last.then_inc(s1_done, 1)

            def project(t, k, segs):
                tok = slice(t * P, (t + 1) * P)
                for y, h in ((y_h, 0), (y_h, 1), (y_l, 0)):
                    for s in segs:
                        last = nc.tensor.matmul(acc2[:, t, s, 0:SEG_N[s]], y[:, k, tok],
                                                w_hl[:, k, h, SEG_AT[s]:SEG_AT[s] + SEG_N[s]],
                                                start=(k == 0 and y is y_h and h == 0),
                                                stop=(k == K - 1 and y is y_l))
                        if s == 0:
                            last0 = last
                return last0 if 0 in segs else last

            def turn(b, t):
                pe.wait_ge(hg_done, b * NT + t + 1)
                nc.tensor.transpose(acc1[:, t, 0:P], hg[:], ident[:]).then_inc(hgT_done, 1)

            def lora(b, t):
                pe.wait_ge(hgT_split, b * NT + t + 1)
                pe.wait_ge(res_split, K + 1)
                for s in range(3):
                    for g, h in ((hgT_h, 0), (hgT_h, 1), (hgT_l, 0)):
                        last = nc.tensor.matmul(acc2[:, t, s, 0:OUT_N[s]], g[:],
                                                b_hl[:, h, OUT_AT[s]:OUT_AT[s] + OUT_N[s]],
                                                start=False, stop=(g is hgT_l), skip_group_check=True)
                    last.then_inc(lora_done, 1)

            def stage2(b):
                for k in range(K):
                    pe.wait_ge(y_split, b * OT + k + 1)
                    pe.wait_ge(res_split, k + 1)
                    last = project(0, k, range(3))
                last.then_inc(seg0_done, 1)
                for k in range(K):
                    last = project(1, k, [0])
                last.then_inc(seg0_done, 1)
                turn(b, 0)
                for k in range(K):
                    project(1, k, [1])
                lora(b, 0)
                turn(b, 1)
                for k in range(K):
                    project(1, k, [2])
                lora(b, 1)

            with pe.Fori(0, NB) as b:
                stage1(b)
                stage2(b)


def kernel(x, itok_B_1_14, itok_B_0_7, L0_cond_weight, L1_cond_W, L1_cond_Wr, L1_cond_A, L1_cond_B):
    import numpy as np
    import concourse.bacc as bacc
    from concourse.bass_utils import run_bass_kernel_spmd

    x, weight, W, Wr, A, B = (np.asarray(a) for a in (x, L0_cond_weight, L1_cond_W, L1_cond_Wr, L1_cond_A, L1_cond_B))
    n_adapters = weight.shape[0]
    xT = x.transpose(0, 2, 1).reshape(NB, K, P, TOK).transpose(0, 2, 1, 3)
    w_adapt = weight.reshape(n_adapters, OT, P, K, P).transpose(0, 1, 4, 3, 2).reshape(n_adapters, OT, P, K * P)
    WT = W.T
    cut = OUT_N[0]
    w_res = np.concatenate([WT[:, :cut], A.reshape(ER, D).T, Wr.T, WT[:, cut:]], axis=1).reshape(K, P, ROW)
    b_lora = B.transpose(0, 2, 1).reshape(ER, D)
    arrays = {
        "xT": xT,
        "adapter_ids": np.asarray(itok_B_1_14).reshape(1, NB),
        "lang_ids": np.broadcast_to(np.asarray(itok_B_0_7), (P, NB)),
        "w_adapt": w_adapt,
        "w_res": w_res,
        "b_lora": b_lora,
    }
    arrays = {name: np.ascontiguousarray(a) for name, a in arrays.items()}

    nc = bacc.Bacc("TRN2", target_bir_lowering=False, num_devices=1)
    aps = [nc.dram_tensor(name, a.shape, mybir.dt.from_np(a.dtype), kind="ExternalInput").ap()
           for name, a in arrays.items()]
    out = nc.dram_tensor("out", (NB, TOK, D), F32, kind="ExternalOutput").ap()
    build(nc, *aps, out)
    got = run_bass_kernel_spmd(nc, [arrays], core_ids=[0])
    return got.results[0]["out"]
```

```python
from contextlib import ExitStack

import concourse.bass as bass
from concourse import mybir

F32 = mybir.dt.float32
F32R = mybir.dt.float32r
I32 = mybir.dt.int32
U32 = mybir.dt.uint32
ALU = mybir.AluOpType
ACT = mybir.ActivationFunctionType

P = 128
NB = 8
TOK = 256
D = 1024
K = D // P
OT = D // P
NE = 8
R = 16
ER = NE * R
NT = TOK // P
LANG_BIAS = 5.0

SEG_AT = [0, 392, 776]
SEG_N = [392, 384, 384]
OUT_AT = [0, 256, 640]
OUT_N = [256, 384, 384]
ROW = sum(SEG_N)
A_AT = 256
R_AT = A_AT + ER

RES = 4
RAW = 4
HL = 4
XP = 4
LOW_BY_GPSIMD = (0, 4, 6, K)
AH = 2
WARM = 14
STEPS = 9


def build(nc, xT, adapter_ids, lang_ids, w_adapt, w_res, b_lora, out):
    with ExitStack() as ctx:
        def sb(name, shape, dt=F32):
            return ctx.enter_context(nc.sbuf_tensor(name, shape, dt))

        def sem(name):
            return ctx.enter_context(nc.semaphore(name))

        w_hl = sb("w_hl", [P, K, 2, ROW], F32R)
        b_hl = sb("b_hl", [P, 2, D], F32R)
        a_raw = sb("a_raw", [P, RAW, K * P])
        a_hl = sb("a_hl", [P, HL, 2, K * P], F32R)
        x_raw = sb("x_raw", [P, K, TOK])
        x_hl = sb("x_hl", [P, K, 2, TOK], F32R)
        y_tmp = sb("y_tmp", [P, 2, TOK])
        y_h = sb("y_h", [P, K, TOK], F32R)
        y_l = sb("y_l", [P, K, TOK], F32R)
        res_raw = sb("res_raw", [P, RES, ROW])
        out_sb = sb("out_sb", [P, NT, D])
        zeros = sb("zeros", [P, 512], mybir.dt.bfloat16)
        ident = sb("ident", [P, P])
        iota8 = sb("iota8", [P, NE])
        iota_be = sb("iota_be", [P, NB, NE])
        lang_sb = sb("lang_sb", [P, NB], I32)
        bias = sb("bias", [P, NB * NE])
        logits = sb("logits", [P, NE])
        top = sb("top", [P, 8])
        top_at = sb("top_at", [P, 8], U32)
        spare = sb("spare", [P, 1])
        e2 = sb("e2", [P, 1])
        half = sb("half", [P, 1])
        p1 = sb("p1", [P, 1])
        p2 = sb("p2", [P, 1])
        g1 = sb("g1", [P, NE])
        g2 = sb("g2", [P, NE])
        gate = sb("gate", [P, NE])
        hg = sb("hg", [P, ER])
        hgT_h = sb("hgT_h", [P, P], F32R)
        hgT_l = sb("hgT_l", [P, P], F32R)

        acc1 = ctx.enter_context(nc.psum_tensor("acc1", [P, 2, 512], F32))
        acc2 = ctx.enter_context(nc.psum_tensor("acc2", [P, NT, 3, 512], F32))

        lang_in = sem("lang_in")
        x_in = [sem(f"x_in{i}") for i in range(XP)]
        a_in = [sem(f"a_in{i}") for i in range(RAW)]
        zeros_set = sem("zeros_set")
        res_in = [sem(f"res_in{i}") for i in range(RES)]
        consts = sem("consts")
        bias_done = sem("bias_done")
        res_diag = sem("res_diag")
        res_high = sem("res_high")
        res_split = [sem(f"res_split{j}") for j in range(K + 1)]
        x_high = sem("x_high")
        x_split = sem("x_split")
        a_high = sem("a_high")
        a_split = sem("a_split")
        s1_done = sem("s1_done")
        y_part = sem("y_part")
        y_sum = sem("y_sum")
        y_high = sem("y_high")
        y_split = sem("y_split")
        seg0_done = sem("seg0_done")
        step = sem("step")
        exp_done = sem("exp_done")
        hg_done = sem("hg_done")
        hgT_done = sem("hgT_done")
        hgT_high = sem("hgT_high")
        hgT_split = sem("hgT_split")
        lora_done = sem("lora_done")
        evac = [sem(f"evac{t}") for t in range(NT)]
        stored = [sem(f"stored{t}") for t in range(NT)]

        def res_parts(j):
            if j < K:
                return w_hl[:, j, 0, :], w_hl[:, j, 1, :], ROW
            return b_hl[:, 0, :], b_hl[:, 1, :], D

        block = ctx.enter_context(nc.Block())

        @block.sync
        def _(sp):
            def load_x(b, pieces=range(XP)):
                for i in pieces:
                    ks = slice(i * K // XP, (i + 1) * K // XP)
                    sp.dma_start(x_raw[:, ks, :], xT[b, :, ks, :]).then_inc(x_in[i], 16)

            def load_a(b, a_id, o):
                if not (isinstance(b, int) and o < RAW):
                    sp.wait_ge(a_split, (b * OT + o - RAW + 1) * AH)
                sp.dma_start(a_raw[:, o % RAW, :], w_adapt[a_id, o]).then_inc(a_in[o % RAW], 16)

            def load_res(j):
                if j >= RES:
                    sp.wait_ge(res_split[j - RES], 1)
                if j < K:
                    sp.dma_start(res_raw[:, j % RES, :], w_res[j]).then_inc(res_in[j % RES], 16)
                else:
                    sp.dma_start(res_raw[:, j % RES, 0:D], b_lora).then_inc(res_in[j % RES], 16)

            def adapter(b):
                return sp.value_load(adapter_ids[0:1, bass.ds(b, 1)], min_val=0, max_val=w_adapt.shape[0] - 1)

            load_x(0, [0])
            a_id = adapter(0)
            load_a(0, a_id, 0)
            load_x(0, range(1, XP))
            for o in range(1, 6):
                load_a(0, a_id, o)
            load_res(0)
            load_a(0, a_id, 6)
            load_res(1)
            sp.dma_start(lang_sb[:], lang_ids).then_inc(lang_in, 16)
            load_a(0, a_id, 7)
            for j in range(2, K + 1):
                load_res(j)
            with sp.Fori(1, NB) as b:
                a_id = adapter(b)
                for o in range(RAW):
                    load_a(b, a_id, o)
                sp.wait_ge(y_sum, b * OT)
                load_x(b)
                for o in range(RAW, OT):
                    load_a(b, a_id, o)

        @block.gpsimd
        def _(pool):
            nc.gpsimd.memset(ident[:], 0.0).then_inc(consts, 1)
            pool.wait_ge(consts, 1)
            nc.gpsimd.affine_select(out=ident[:], in_=ident[:], compare_op=ALU.not_equal, fill=1.0, base=0,
                                    pattern=[[-1, P]], channel_multiplier=1).then_inc(consts, 1)
            nc.gpsimd.iota(iota8[:], pattern=[[1, NE]], base=0, channel_multiplier=0,
                           allow_small_or_imprecise_dtypes=True).then_inc(consts, 1)
            nc.gpsimd.iota(iota_be[:], pattern=[[0, NB], [1, NE]], base=0, channel_multiplier=0,
                           allow_small_or_imprecise_dtypes=True).then_inc(consts, 1)
            pool.wait_ge(consts, 4)

            def add_identity(j):
                pool.wait_ge(res_in[j % RES], 16 * (j // RES + 1))
                at = j * P if j * P < OUT_N[0] else SEG_AT[1] - OUT_AT[1] + j * P
                diag = res_raw[:, j % RES, at:at + P]
                nc.gpsimd.tensor_tensor(diag, diag, ident[:], ALU.add).then_inc(res_diag, 1)

            def low_res(j):
                pool.wait_ge(res_high, j + 1)
                high, low, n = res_parts(j)
                nc.gpsimd.tensor_tensor(low, res_raw[:, j % RES, 0:n], high.bitcast(F32),
                                        ALU.subtract).then_inc(res_split[j], 1)

            add_identity(0)
            add_identity(1)
            low_res(0)
            for j in range(2, 6):
                add_identity(j)
            low_res(4)
            add_identity(6)
            add_identity(7)
            low_res(6)
            low_res(K)

        @block.scalar
        def _(act):
            def high_x(b, pieces=range(XP)):
                for i in pieces:
                    ks = slice(i * K // XP, (i + 1) * K // XP)
                    act.wait_ge(x_in[i], 16 * b + 16)
                    if i == 0 and not (isinstance(b, int) and b == 0):
                        act.wait_ge(s1_done, b * OT)
                    nc.scalar.copy(x_hl[:, ks, 0, :], x_raw[:, ks, :]).then_inc(x_high, 1)

            def high_a(b, o):
                act.wait_ge(a_in[o % RAW], 16 * (b * (OT // RAW) + o // RAW + 1))
                if not (isinstance(b, int) and b == 0 and o < HL):
                    act.wait_ge(s1_done, b * OT + o - HL + 1)
                for h in range(AH):
                    at = slice(h * K * P // AH, (h + 1) * K * P // AH)
                    nc.scalar.copy(a_hl[:, o % HL, 0, at], a_raw[:, o % RAW, at]).then_inc(a_high, 1)

            def high_res(j):
                if j < K:
                    act.wait_ge(res_diag, j + 1)
                else:
                    act.wait_ge(res_in[j % RES], 16 * (j // RES + 1))
                high, _, n = res_parts(j)
                nc.scalar.copy(high, res_raw[:, j % RES, 0:n]).then_inc(res_high, 1)

            def stage1(b, first=False):
                for o in range(OT):
                    if first and o == 0:
                        high_a(b, HL - 1)
                    if o + HL < OT:
                        high_a(b, o + HL)
                    act.wait_ge(y_sum, b * OT + o + 1)
                    nc.scalar.copy(y_h[:, o, :], y_tmp[:, o % 2, :]).then_inc(y_high, 1)
                    if first and o >= 1:
                        high_res(o - 1)
                if first:
                    for j in range(OT - 1, K + 1):
                        high_res(j)

            def weight_of_second(b, t):
                act.wait_ge(step, STEPS * (b * NT + t) + 2)
                nc.scalar.activation(e2[:], top[:, 0:1], ACT.Exp, bias=top[:, 1:2],
                                     scale=-1.0).then_inc(exp_done, 1)

            def high_hgT(b, t):
                act.wait_ge(hgT_done, b * NT + t + 1)
                nc.scalar.copy(hgT_h[:], acc1[:, t, 0:P]).then_inc(hgT_high, 1)

            def result(b, t):
                if not (isinstance(b, int) and b == 0):
                    act.wait_ge(stored[t], b * 32)
                for s in range(3):
                    act.wait_ge(lora_done, (b * NT + t) * 3 + s + 1)
                    at = slice(OUT_AT[s], OUT_AT[s] + OUT_N[s])
                    nc.scalar.copy(out_sb[:, t, at], acc2[:, t, s, 0:OUT_N[s]]).then_inc(evac[t], 1)
                    if s > 0:
                        part = slice(0, OUT_AT[2]) if s == 1 else at
                        act.wait_ge(evac[t], b * 3 + s + 1)
                        act.dma_start(out[b, t * P:(t + 1) * P, part], out_sb[:, t, part]).then_inc(stored[t], 16)

            def stage2(b, last=False):
                if not last:
                    for o in range(HL):
                        high_a(b + 1, o)
                weight_of_second(b, 0)
                high_hgT(b, 0)
                if not last:
                    high_x(b + 1, range(XP // 2))
                weight_of_second(b, 1)
                high_hgT(b, 1)
                if not last:
                    high_x(b + 1, range(XP // 2, XP))
                result(b, 0)
                result(b, 1)

            high_x(0, [0])
            high_a(0, 0)
            high_x(0, range(1, XP))
            for o in range(1, HL - 1):
                high_a(0, o)
            stage1(0, first=True)
            stage2(0)
            with act.Fori(1, NB - 1) as b:
                stage1(b)
                stage2(b)
            stage1(NB - 1)
            stage2(NB - 1, last=True)
            for t in range(NT):
                act.wait_ge(stored[t], 32 * NB)

        @block.vector
        def _(dve):
            def low_x(b, pieces=range(XP)):
                for i in pieces:
                    ks = slice(i * K // XP, (i + 1) * K // XP)
                    dve.wait_ge(x_high, b * XP + i + 1)
                    nc.vector.tensor_tensor(x_hl[:, ks, 1, :], x_raw[:, ks, :], x_hl[:, ks, 0, :].bitcast(F32),
                                            ALU.subtract).then_inc(x_split, 1)

            def low_a(b, o):
                for h in range(AH):
                    at = slice(h * K * P // AH, (h + 1) * K * P // AH)
                    dve.wait_ge(a_high, (b * OT + o) * AH + h + 1)
                    nc.vector.tensor_tensor(a_hl[:, o % HL, 1, at], a_raw[:, o % RAW, at],
                                            a_hl[:, o % HL, 0, at].bitcast(F32), ALU.subtract).then_inc(a_split, 1)

            def low_res(j):
                dve.wait_ge(res_high, j + 1)
                high, low, n = res_parts(j)
                nc.vector.tensor_tensor(low, res_raw[:, j % RES, 0:n], high.bitcast(F32),
                                        ALU.subtract).then_inc(res_split[j], 1)

            def stage1(b, first=False):
                for o in range(OT):
                    y = y_tmp[:, o % 2, :]
                    dve.wait_ge(s1_done, b * OT + o + 1)
                    nc.vector.tensor_tensor(y, acc1[:, o % 2, 0:TOK], x_raw[:, o, :], ALU.add).then_inc(y_part, 1)
                    dve.wait_ge(y_part, b * OT + o + 1)
                    nc.vector.tensor_tensor(y, acc1[:, o % 2, TOK:2 * TOK], y, ALU.add).then_inc(y_sum, 1)
                    if first and o == 0:
                        low_a(b, HL - 1)
                    if o + HL < OT:
                        low_a(b, o + HL)
                    dve.wait_ge(y_high, b * OT + o + 1)
                    nc.vector.tensor_tensor(y_l[:, o, :], y, y_h[:, o, :].bitcast(F32),
                                            ALU.subtract).then_inc(y_split, 1)
                    if first and o >= 2 and o - 2 not in LOW_BY_GPSIMD:
                        low_res(o - 2)
                if first:
                    for j in range(OT - 2, K):
                        if j not in LOW_BY_GPSIMD:
                            low_res(j)

            def gates(b, t):
                base = STEPS * (b * NT + t)
                dve.wait_ge(seg0_done, b * NT + t + 1)
                nc.vector.tensor_tensor(logits[:], acc2[:, t, 0, R_AT:R_AT + NE],
                                        bias[:, bass.ds(b * NE, NE)], ALU.add).then_inc(step, 1)
                dve.wait_ge(step, base + 1)
                nc.vector.memset(spare[:], 0.0)
                nc.vector.max(top[:], logits[:]).then_inc(step, 1)
                dve.wait_ge(step, base + 2)
                nc.vector.memset(spare[:], 0.0)
                nc.vector.max_index(top_at[:], top[:], logits[:]).then_inc(step, 1)
                dve.wait_ge(exp_done, b * NT + t + 1)
                nc.vector.tensor_scalar(half[:], e2[:], 1.0, 0.5, ALU.add, ALU.mult).then_inc(step, 1)
                dve.wait_ge(step, base + 4)
                nc.vector.reciprocal(p1[:], half[:]).then_inc(step, 1)
                dve.wait_ge(step, base + 5)
                nc.vector.tensor_tensor(p2[:], p1[:], e2[:], ALU.mult).then_inc(step, 1)
                nc.vector.scalar_tensor_tensor(out=g1[:], in0=iota8[:], scalar=top_at[:, 0:1],
                                               in1=p1[:].to_broadcast([P, NE]), op0=ALU.is_equal,
                                               op1=ALU.mult).then_inc(step, 1)
                dve.wait_ge(step, base + 6)
                nc.vector.scalar_tensor_tensor(out=g2[:], in0=iota8[:], scalar=top_at[:, 1:2],
                                               in1=p2[:].to_broadcast([P, NE]), op0=ALU.is_equal,
                                               op1=ALU.mult).then_inc(step, 1)
                dve.wait_ge(step, base + 8)
                nc.vector.tensor_tensor(gate[:], g1[:], g2[:], ALU.add).then_inc(step, 1)
                dve.wait_ge(step, base + 9)
                nc.vector.tensor_tensor(hg[:].rearrange("p (e r) -> p e r", e=NE),
                                        acc2[:, t, 0, A_AT:A_AT + ER].rearrange("p (e r) -> p e r", e=NE),
                                        gate[:].rearrange("p (e r) -> p e r", r=1).to_broadcast([P, NE, R]),
                                        ALU.mult).then_inc(hg_done, 1)

            def low_hgT(b, t):
                dve.wait_ge(hgT_high, b * NT + t + 1)
                nc.vector.tensor_tensor(hgT_l[:], acc1[:, t, 0:P], hgT_h[:].bitcast(F32),
                                        ALU.subtract).then_inc(hgT_split, 1)

            def stage2(b, last=False):
                if not last:
                    for o in range(HL):
                        low_a(b + 1, o)
                gates(b, 0)
                low_hgT(b, 0)
                if not last:
                    low_x(b + 1, range(XP // 2))
                gates(b, 1)
                low_hgT(b, 1)
                if not last:
                    low_x(b + 1, range(XP // 2, XP))

            nc.vector.memset(zeros[:], 0.0).then_inc(zeros_set, 1)
            low_x(0, [0])
            low_a(0, 0)
            low_x(0, range(1, XP))
            for o in range(1, HL - 1):
                low_a(0, o)
            stage1(0, first=True)
            dve.wait_ge(consts, 4)
            dve.wait_ge(lang_in, 16)
            nc.vector.tensor_tensor(bias[:].rearrange("p (b e) -> p b e", b=NB), iota_be[:],
                                    lang_sb[:].rearrange("p (b e) -> p b e", e=1).to_broadcast([P, NB, NE]),
                                    ALU.is_equal).then_inc(bias_done, 1)
            dve.wait_ge(bias_done, 1)
            nc.vector.tensor_scalar(bias[:], bias[:], LANG_BIAS, None, ALU.mult).then_inc(bias_done, 1)
            dve.wait_ge(bias_done, 2)
            stage2(0)
            with dve.Fori(1, NB - 1) as b:
                stage1(b)
                stage2(b)
            stage1(NB - 1)
            stage2(NB - 1, last=True)

        @block.tensor
        def _(pe):
            def stage1(b):
                for o in range(OT):
                    if o >= 2:
                        pe.wait_ge(y_sum, b * OT + o - 1)
                    for k in range(K):
                        if k % (K // AH) == 0:
                            pe.wait_ge(a_split, (b * OT + o) * AH + k // (K // AH) + 1)
                        if o == 0 and k % (K // XP) == 0:
                            pe.wait_ge(x_split, b * XP + k // (K // XP) + 1)
                        ko = slice(k * P, (k + 1) * P)
                        nc.tensor.matmul(acc1[:, o % 2, :], a_hl[:, o % HL, 0, ko],
                                         x_hl[:, k, :, :].rearrange("p h n -> p (h n)"),
                                         start=(k == 0), stop=False)
                        last = nc.tensor.matmul(acc1[:, o % 2, 0:TOK], a_hl[:, o % HL, 1, ko],
                                                x_hl[:, k, 0, :], start=False, stop=(k == K - 1))
                    last.then_inc(s1_done, 1)

            def project(t, k, segs):
                tok = slice(t * P, (t + 1) * P)
                for y, h in ((y_h, 0), (y_h, 1), (y_l, 0)):
                    for s in segs:
                        last = nc.tensor.matmul(acc2[:, t, s, 0:SEG_N[s]], y[:, k, tok],
                                                w_hl[:, k, h, SEG_AT[s]:SEG_AT[s] + SEG_N[s]],
                                                start=(k == 0 and y is y_h and h == 0),
                                                stop=(k == K - 1 and y is y_l))
                        if s == 0:
                            last0 = last
                return last0 if 0 in segs else last

            def turn(b, t):
                pe.wait_ge(hg_done, b * NT + t + 1)
                nc.tensor.transpose(acc1[:, t, 0:P], hg[:], ident[:]).then_inc(hgT_done, 1)

            def lora(b, t):
                pe.wait_ge(hgT_split, b * NT + t + 1)
                pe.wait_ge(res_split[K], 1)
                for s in range(3):
                    for g, h in ((hgT_h, 0), (hgT_h, 1), (hgT_l, 0)):
                        last = nc.tensor.matmul(acc2[:, t, s, 0:OUT_N[s]], g[:],
                                                b_hl[:, h, OUT_AT[s]:OUT_AT[s] + OUT_N[s]],
                                                start=False, stop=(g is hgT_l), skip_group_check=True)
                    last.then_inc(lora_done, 1)

            def stage2(b):
                for k in range(K):
                    pe.wait_ge(y_split, b * OT + k + 1)
                    pe.wait_ge(res_split[k], 1)
                    last = project(0, k, range(3))
                last.then_inc(seg0_done, 1)
                for k in range(K):
                    last = project(1, k, [0])
                last.then_inc(seg0_done, 1)
                turn(b, 0)
                for k in range(K):
                    project(1, k, [1])
                lora(b, 0)
                turn(b, 1)
                for k in range(K):
                    project(1, k, [2])
                lora(b, 1)

            pe.wait_ge(zeros_set, 1)
            for _ in range(WARM):
                nc.tensor.matmul(acc2[:, 0, 0, :], zeros[:, 0:P], zeros[:], start=True, stop=True)
            with pe.Fori(0, NB) as b:
                stage1(b)
                stage2(b)


def kernel(x, itok_B_1_14, itok_B_0_7, L0_cond_weight, L1_cond_W, L1_cond_Wr, L1_cond_A, L1_cond_B):
    import numpy as np
    import concourse.bacc as bacc
    from concourse.bass_utils import run_bass_kernel_spmd

    x, weight, W, Wr, A, B = (np.asarray(a) for a in (x, L0_cond_weight, L1_cond_W, L1_cond_Wr, L1_cond_A, L1_cond_B))
    n_adapters = weight.shape[0]
    xT = x.transpose(0, 2, 1).reshape(NB, K, P, TOK).transpose(0, 2, 1, 3)
    w_adapt = weight.reshape(n_adapters, OT, P, K, P).transpose(0, 1, 4, 3, 2).reshape(n_adapters, OT, P, K * P)
    WT = W.T
    cut = OUT_N[0]
    w_res = np.concatenate([WT[:, :cut], A.reshape(ER, D).T, Wr.T, WT[:, cut:]], axis=1).reshape(K, P, ROW)
    b_lora = B.transpose(0, 2, 1).reshape(ER, D)
    arrays = {
        "xT": xT,
        "adapter_ids": np.asarray(itok_B_1_14).reshape(1, NB),
        "lang_ids": np.broadcast_to(np.asarray(itok_B_0_7), (P, NB)),
        "w_adapt": w_adapt,
        "w_res": w_res,
        "b_lora": b_lora,
    }
    arrays = {name: np.ascontiguousarray(a) for name, a in arrays.items()}

    nc = bacc.Bacc("TRN2", target_bir_lowering=False, num_devices=1)
    aps = [nc.dram_tensor(name, a.shape, mybir.dt.from_np(a.dtype), kind="ExternalInput").ap()
           for name, a in arrays.items()]
    out = nc.dram_tensor("out", (NB, TOK, D), F32, kind="ExternalOutput").ap()
    build(nc, *aps, out)
    got = run_bass_kernel_spmd(nc, [arrays], core_ids=[0])
    return got.results[0]["out"]
```

```python
from contextlib import ExitStack

import concourse.bass as bass
from concourse import mybir

F32 = mybir.dt.float32
F32R = mybir.dt.float32r
I32 = mybir.dt.int32
U32 = mybir.dt.uint32
ALU = mybir.AluOpType
ACT = mybir.ActivationFunctionType

P = 128
NB = 8
TOK = 256
D = 1024
K = D // P
OT = D // P
NE = 8
R = 16
ER = NE * R
NT = TOK // P
LANG_BIAS = 5.0

SEG_AT = [0, 392, 776]
SEG_N = [392, 384, 384]
OUT_AT = [0, 256, 640]
OUT_N = [256, 384, 384]
ROW = sum(SEG_N)
A_AT = 256
R_AT = A_AT + ER

RES = 5
RAW = 4
HL = 4
XP = 4
AH = 2
HIGH_RES = 2
LOW_RES = 4
WARM = 13
STEPS = 9


def build(nc, xT, adapter_ids, lang_ids, w_adapt, w_res, b_lora, out):
    with ExitStack() as ctx:
        def sb(name, shape, dt=F32):
            return ctx.enter_context(nc.sbuf_tensor(name, shape, dt))

        def sem(name):
            return ctx.enter_context(nc.semaphore(name))

        w_hl = sb("w_hl", [P, K, 2, ROW], F32R)
        b_hl = sb("b_hl", [P, 2, D], F32R)
        a_raw = sb("a_raw", [P, RAW, K * P])
        a_hl = sb("a_hl", [P, HL, 2, K * P], F32R)
        x_raw = sb("x_raw", [P, K, TOK])
        x_hl = sb("x_hl", [P, K, 2, TOK], F32R)
        y_tmp = sb("y_tmp", [P, 2, TOK])
        y_h = sb("y_h", [P, K, TOK], F32R)
        y_l = sb("y_l", [P, K, TOK], F32R)
        res_raw = sb("res_raw", [P, RES, ROW])
        out_sb = sb("out_sb", [P, NT, D])
        zeros = sb("zeros", [P, 512], mybir.dt.bfloat16)
        ident = sb("ident", [P, P])
        iota8 = sb("iota8", [P, NE])
        iota_be = sb("iota_be", [P, NB, NE])
        lang_sb = sb("lang_sb", [P, NB], I32)
        bias = sb("bias", [P, NB * NE])
        logits = sb("logits", [P, NE])
        top = sb("top", [P, 8])
        top_at = sb("top_at", [P, 8], U32)
        spare = sb("spare", [P, 1])
        e2 = sb("e2", [P, 1])
        half = sb("half", [P, 1])
        p1 = sb("p1", [P, 1])
        p2 = sb("p2", [P, 1])
        g1 = sb("g1", [P, NE])
        g2 = sb("g2", [P, NE])
        gate = sb("gate", [P, NE])
        hg = sb("hg", [P, ER])
        hgT_h = sb("hgT_h", [P, P], F32R)
        hgT_l = sb("hgT_l", [P, P], F32R)

        acc1 = ctx.enter_context(nc.psum_tensor("acc1", [P, 2, 512], F32))
        acc2 = ctx.enter_context(nc.psum_tensor("acc2", [P, NT, 3, 512], F32))

        lang_in = sem("lang_in")
        x_in = [sem(f"x_in{i}") for i in range(XP)]
        a_in = [sem(f"a_in{i}") for i in range(RAW)]
        zeros_set = sem("zeros_set")
        b_in = sem("b_in")
        res_in = [sem(f"res_in{i}") for i in range(RES)]
        consts = sem("consts")
        bias_done = sem("bias_done")
        res_diag = sem("res_diag")
        res_high = sem("res_high")
        res_split = [sem(f"res_split{j}") for j in range(K + 1)]
        x_high = sem("x_high")
        x_split = sem("x_split")
        a_first = sem("a_first")
        a_high = sem("a_high")
        a_split = sem("a_split")
        s1_done = sem("s1_done")
        y_part = sem("y_part")
        y_sum = sem("y_sum")
        y_high = sem("y_high")
        y_split = sem("y_split")
        seg0_done = sem("seg0_done")
        step = sem("step")
        exp_done = sem("exp_done")
        hg_done = sem("hg_done")
        hgT_done = sem("hgT_done")
        hgT_high = sem("hgT_high")
        hgT_split = sem("hgT_split")
        lora_done = sem("lora_done")
        evac = [sem(f"evac{t}") for t in range(NT)]
        stored = [sem(f"stored{t}") for t in range(NT)]

        def res_parts(j):
            if j < K:
                return res_raw[:, j % RES, :], w_hl[:, j, 0, :], w_hl[:, j, 1, :]
            return out_sb[:, 0, :], b_hl[:, 0, :], b_hl[:, 1, :]

        block = ctx.enter_context(nc.Block())

        @block.sync
        def _(sp):
            def load_x(b, pieces=range(XP)):
                for i in pieces:
                    ks = slice(i * K // XP, (i + 1) * K // XP)
                    sp.dma_start(x_raw[:, ks, :], xT[b, :, ks, :]).then_inc(x_in[i], 16)

            def load_a(b, a_id, o):
                if not (isinstance(b, int) and o < RAW):
                    sp.wait_ge(a_split, (b * OT + o - RAW + 1) * AH)
                sp.dma_start(a_raw[:, o % RAW, :], w_adapt[a_id, o]).then_inc(a_in[o % RAW], 16)

            def load_res(j):
                if RES <= j < K:
                    sp.wait_ge(res_split[j - RES], 1)
                if j < K:
                    sp.dma_start(res_raw[:, j % RES, :], w_res[j]).then_inc(res_in[j % RES], 16)
                else:
                    sp.dma_start(out_sb[:, 0, :], b_lora).then_inc(b_in, 16)

            def adapter(b):
                return sp.value_load(adapter_ids[0:1, bass.ds(b, 1)], min_val=0, max_val=w_adapt.shape[0] - 1)

            load_x(0, [0])
            a_id = adapter(0)
            half_row = K * P // AH
            sp.dma_start(a_raw[:, 0, 0:half_row], w_adapt[a_id, 0, :, 0:half_row]).then_inc(a_first, 16)
            sp.dma_start(a_raw[:, 0, half_row:], w_adapt[a_id, 0, :, half_row:]).then_inc(a_in[0], 16)
            load_x(0, range(1, XP))
            for o in range(1, OT - 2):
                load_a(0, a_id, o)
            load_res(0)
            load_a(0, a_id, OT - 2)
            load_res(1)
            sp.dma_start(lang_sb[:], lang_ids).then_inc(lang_in, 16)
            load_a(0, a_id, OT - 1)
            for j in range(2, K + 1):
                load_res(j)
            with sp.Fori(1, NB) as b:
                a_id = adapter(b)
                for o in range(RAW):
                    load_a(b, a_id, o)
                sp.wait_ge(y_sum, b * OT)
                load_x(b)
                for o in range(RAW, OT):
                    load_a(b, a_id, o)

        @block.gpsimd
        def _(pool):
            nc.gpsimd.memset(ident[:], 0.0).then_inc(consts, 1)
            pool.wait_ge(consts, 1)
            nc.gpsimd.affine_select(out=ident[:], in_=ident[:], compare_op=ALU.not_equal, fill=1.0, base=0,
                                    pattern=[[-1, P]], channel_multiplier=1).then_inc(consts, 1)
            nc.gpsimd.iota(iota8[:], pattern=[[1, NE]], base=0, channel_multiplier=0,
                           allow_small_or_imprecise_dtypes=True).then_inc(consts, 1)
            nc.gpsimd.iota(iota_be[:], pattern=[[0, NB], [1, NE]], base=0, channel_multiplier=0,
                           allow_small_or_imprecise_dtypes=True).then_inc(consts, 1)
            pool.wait_ge(consts, 4)

            def add_identity(j):
                pool.wait_ge(res_in[j % RES], 16 * (j // RES + 1))
                at = j * P if j * P < OUT_N[0] else SEG_AT[1] - OUT_AT[1] + j * P
                diag = res_raw[:, j % RES, at:at + P]
                nc.gpsimd.tensor_tensor(diag, diag, ident[:], ALU.add).then_inc(res_diag, 1)

            for j in range(K):
                add_identity(j)

        @block.scalar
        def _(act):
            def high_x(b, pieces=range(XP)):
                for i in pieces:
                    ks = slice(i * K // XP, (i + 1) * K // XP)
                    act.wait_ge(x_in[i], 16 * b + 16)
                    if i == 0 and not (isinstance(b, int) and b == 0):
                        act.wait_ge(s1_done, b * OT)
                    nc.scalar.copy(x_hl[:, ks, 0, :], x_raw[:, ks, :]).then_inc(x_high, 1)

            def high_a(b, o):
                first = isinstance(b, int) and b == 0 and o == 0
                if first:
                    act.wait_ge(a_first, 16)
                else:
                    act.wait_ge(a_in[o % RAW], 16 * (b * (OT // RAW) + o // RAW + 1))
                if not (isinstance(b, int) and b == 0 and o < HL):
                    act.wait_ge(s1_done, b * OT + o - HL + 1)
                for h in range(AH):
                    at = slice(h * K * P // AH, (h + 1) * K * P // AH)
                    if first and h == 1:
                        act.wait_ge(a_in[0], 16)
                    nc.scalar.copy(a_hl[:, o % HL, 0, at], a_raw[:, o % RAW, at]).then_inc(a_high, 1)

            def high_res(j):
                if j < K:
                    act.wait_ge(res_diag, j + 1)
                else:
                    act.wait_ge(b_in, 16)
                raw, high, _ = res_parts(j)
                nc.scalar.copy(high, raw).then_inc(res_high, 1)

            def stage1(b, first=False):
                ahead = HL - 1 if first else HL
                for o in range(OT):
                    if o + ahead < OT:
                        high_a(b, o + ahead)
                    act.wait_ge(y_sum, b * OT + o + 1)
                    nc.scalar.copy(y_h[:, o, :], y_tmp[:, o % 2, :]).then_inc(y_high, 1)
                    if first and o >= HIGH_RES:
                        high_res(o - HIGH_RES)
                if first:
                    for j in range(OT - HIGH_RES, K + 1):
                        high_res(j)

            def weight_of_second(b, t):
                act.wait_ge(step, STEPS * (b * NT + t) + 2)
                nc.scalar.activation(e2[:], top[:, 0:1], ACT.Exp, bias=top[:, 1:2],
                                     scale=-1.0).then_inc(exp_done, 1)

            def high_hgT(b, t):
                act.wait_ge(hgT_done, b * NT + t + 1)
                nc.scalar.copy(hgT_h[:], acc1[:, t, 0:P]).then_inc(hgT_high, 1)

            def result(b, t):
                if not (isinstance(b, int) and b == 0):
                    act.wait_ge(stored[t], b * 32)
                for s in range(3):
                    act.wait_ge(lora_done, (b * NT + t) * 3 + s + 1)
                    at = slice(OUT_AT[s], OUT_AT[s] + OUT_N[s])
                    nc.scalar.copy(out_sb[:, t, at], acc2[:, t, s, 0:OUT_N[s]]).then_inc(evac[t], 1)
                    if s > 0:
                        part = slice(0, OUT_AT[2]) if s == 1 else at
                        act.wait_ge(evac[t], b * 3 + s + 1)
                        act.dma_start(out[b, t * P:(t + 1) * P, part], out_sb[:, t, part]).then_inc(stored[t], 16)

            def stage2(b, last=False):
                if not last:
                    for o in range(HL - 1):
                        high_a(b + 1, o)
                weight_of_second(b, 0)
                high_hgT(b, 0)
                if not last:
                    high_a(b + 1, HL - 1)
                weight_of_second(b, 1)
                high_hgT(b, 1)
                if not last:
                    high_x(b + 1)
                result(b, 0)
                result(b, 1)

            high_x(0, [0])
            high_a(0, 0)
            high_x(0, range(1, XP))
            for o in range(1, HL - 1):
                high_a(0, o)
            stage1(0, first=True)
            stage2(0)
            with act.Fori(1, NB - 1) as b:
                stage1(b)
                stage2(b)
            stage1(NB - 1)
            stage2(NB - 1, last=True)
            for t in range(NT):
                act.wait_ge(stored[t], 32 * NB)

        @block.vector
        def _(dve):
            def low_x(b, pieces=range(XP)):
                for i in pieces:
                    ks = slice(i * K // XP, (i + 1) * K // XP)
                    dve.wait_ge(x_high, b * XP + i + 1)
                    nc.vector.tensor_tensor(x_hl[:, ks, 1, :], x_raw[:, ks, :], x_hl[:, ks, 0, :].bitcast(F32),
                                            ALU.subtract).then_inc(x_split, 1)

            def low_a(b, o):
                for h in range(AH):
                    at = slice(h * K * P // AH, (h + 1) * K * P // AH)
                    dve.wait_ge(a_high, (b * OT + o) * AH + h + 1)
                    nc.vector.tensor_tensor(a_hl[:, o % HL, 1, at], a_raw[:, o % RAW, at],
                                            a_hl[:, o % HL, 0, at].bitcast(F32), ALU.subtract).then_inc(a_split, 1)

            def low_res(j):
                dve.wait_ge(res_high, j + 1)
                raw, high, low = res_parts(j)
                nc.vector.tensor_tensor(low, raw, high.bitcast(F32),
                                        ALU.subtract).then_inc(res_split[j], 1)

            def stage1(b, first=False):
                ahead = HL - 1 if first else HL
                for o in range(OT):
                    y = y_tmp[:, o % 2, :]
                    dve.wait_ge(s1_done, b * OT + o + 1)
                    nc.vector.tensor_tensor(y, acc1[:, o % 2, 0:TOK], x_raw[:, o, :], ALU.add).then_inc(y_part, 1)
                    dve.wait_ge(y_part, b * OT + o + 1)
                    nc.vector.tensor_tensor(y, acc1[:, o % 2, TOK:2 * TOK], y, ALU.add).then_inc(y_sum, 1)
                    if o + ahead < OT:
                        low_a(b, o + ahead)
                    if first and o >= LOW_RES:
                        low_res(o - LOW_RES)
                    dve.wait_ge(y_high, b * OT + o + 1)
                    nc.vector.tensor_tensor(y_l[:, o, :], y, y_h[:, o, :].bitcast(F32),
                                            ALU.subtract).then_inc(y_split, 1)
                if first:
                    for j in range(OT - LOW_RES, K + 1):
                        low_res(j)

            def gates(b, t):
                base = STEPS * (b * NT + t)
                dve.wait_ge(seg0_done, b * NT + t + 1)
                nc.vector.tensor_tensor(logits[:], acc2[:, t, 0, R_AT:R_AT + NE],
                                        bias[:, bass.ds(b * NE, NE)], ALU.add).then_inc(step, 1)
                dve.wait_ge(step, base + 1)
                nc.vector.memset(spare[:], 0.0)
                nc.vector.max(top[:], logits[:]).then_inc(step, 1)
                dve.wait_ge(step, base + 2)
                nc.vector.memset(spare[:], 0.0)
                nc.vector.max_index(top_at[:], top[:], logits[:]).then_inc(step, 1)
                dve.wait_ge(exp_done, b * NT + t + 1)
                nc.vector.tensor_scalar(half[:], e2[:], 1.0, 0.5, ALU.add, ALU.mult).then_inc(step, 1)
                dve.wait_ge(step, base + 4)
                nc.vector.reciprocal(p1[:], half[:]).then_inc(step, 1)
                dve.wait_ge(step, base + 5)
                nc.vector.tensor_tensor(p2[:], p1[:], e2[:], ALU.mult).then_inc(step, 1)
                nc.vector.scalar_tensor_tensor(out=g1[:], in0=iota8[:], scalar=top_at[:, 0:1],
                                               in1=p1[:].to_broadcast([P, NE]), op0=ALU.is_equal,
                                               op1=ALU.mult).then_inc(step, 1)
                dve.wait_ge(step, base + 6)
                nc.vector.scalar_tensor_tensor(out=g2[:], in0=iota8[:], scalar=top_at[:, 1:2],
                                               in1=p2[:].to_broadcast([P, NE]), op0=ALU.is_equal,
                                               op1=ALU.mult).then_inc(step, 1)
                dve.wait_ge(step, base + 8)
                nc.vector.tensor_tensor(gate[:], g1[:], g2[:], ALU.add).then_inc(step, 1)
                dve.wait_ge(step, base + 9)
                nc.vector.tensor_tensor(hg[:].rearrange("p (e r) -> p e r", e=NE),
                                        acc2[:, t, 0, A_AT:A_AT + ER].rearrange("p (e r) -> p e r", e=NE),
                                        gate[:].rearrange("p (e r) -> p e r", r=1).to_broadcast([P, NE, R]),
                                        ALU.mult).then_inc(hg_done, 1)

            def low_hgT(b, t):
                dve.wait_ge(hgT_high, b * NT + t + 1)
                nc.vector.tensor_tensor(hgT_l[:], acc1[:, t, 0:P], hgT_h[:].bitcast(F32),
                                        ALU.subtract).then_inc(hgT_split, 1)

            def stage2(b, last=False):
                if not last:
                    for o in range(HL - 1):
                        low_a(b + 1, o)
                gates(b, 0)
                low_hgT(b, 0)
                if not last:
                    low_a(b + 1, HL - 1)
                gates(b, 1)
                low_hgT(b, 1)
                if not last:
                    low_x(b + 1)

            nc.vector.memset(zeros[:], 0.0).then_inc(zeros_set, 1)
            low_x(0, [0])
            low_a(0, 0)
            low_x(0, range(1, XP))
            for o in range(1, HL - 1):
                low_a(0, o)
            stage1(0, first=True)
            dve.wait_ge(consts, 4)
            dve.wait_ge(lang_in, 16)
            nc.vector.tensor_tensor(bias[:].rearrange("p (b e) -> p b e", b=NB), iota_be[:],
                                    lang_sb[:].rearrange("p (b e) -> p b e", e=1).to_broadcast([P, NB, NE]),
                                    ALU.is_equal).then_inc(bias_done, 1)
            dve.wait_ge(bias_done, 1)
            nc.vector.tensor_scalar(bias[:], bias[:], LANG_BIAS, None, ALU.mult).then_inc(bias_done, 1)
            dve.wait_ge(bias_done, 2)
            stage2(0)
            with dve.Fori(1, NB - 1) as b:
                stage1(b)
                stage2(b)
            stage1(NB - 1)
            stage2(NB - 1, last=True)

        @block.tensor
        def _(pe):
            def stage1(b):
                for o in range(OT):
                    if o >= 2:
                        pe.wait_ge(y_sum, b * OT + o - 1)
                    for k in range(K):
                        if k % (K // AH) == 0:
                            pe.wait_ge(a_split, (b * OT + o) * AH + k // (K // AH) + 1)
                        if o == 0 and k % (K // XP) == 0:
                            pe.wait_ge(x_split, b * XP + k // (K // XP) + 1)
                        ko = slice(k * P, (k + 1) * P)
                        nc.tensor.matmul(acc1[:, o % 2, :], a_hl[:, o % HL, 0, ko],
                                         x_hl[:, k, :, :].rearrange("p h n -> p (h n)"),
                                         start=(k == 0), stop=False)
                        last = nc.tensor.matmul(acc1[:, o % 2, 0:TOK], a_hl[:, o % HL, 1, ko],
                                                x_hl[:, k, 0, :], start=False, stop=(k == K - 1))
                    last.then_inc(s1_done, 1)

            def project(t, k, segs):
                tok = slice(t * P, (t + 1) * P)
                for y, h in ((y_h, 0), (y_h, 1), (y_l, 0)):
                    for s in segs:
                        last = nc.tensor.matmul(acc2[:, t, s, 0:SEG_N[s]], y[:, k, tok],
                                                w_hl[:, k, h, SEG_AT[s]:SEG_AT[s] + SEG_N[s]],
                                                start=(k == 0 and y is y_h and h == 0),
                                                stop=(k == K - 1 and y is y_l))
                        if s == 0:
                            last0 = last
                return last0 if 0 in segs else last

            def turn(b, t):
                pe.wait_ge(hg_done, b * NT + t + 1)
                nc.tensor.transpose(acc1[:, t, 0:P], hg[:], ident[:]).then_inc(hgT_done, 1)

            def lora(b, t):
                pe.wait_ge(hgT_split, b * NT + t + 1)
                pe.wait_ge(res_split[K], 1)
                for s in range(3):
                    for g, h in ((hgT_h, 0), (hgT_h, 1), (hgT_l, 0)):
                        last = nc.tensor.matmul(acc2[:, t, s, 0:OUT_N[s]], g[:],
                                                b_hl[:, h, OUT_AT[s]:OUT_AT[s] + OUT_N[s]],
                                                start=False, stop=(g is hgT_l), skip_group_check=True)
                    last.then_inc(lora_done, 1)

            def stage2(b):
                for k in range(K):
                    pe.wait_ge(y_split, b * OT + k + 1)
                    pe.wait_ge(res_split[k], 1)
                    last = project(0, k, range(3))
                last.then_inc(seg0_done, 1)
                for k in range(K):
                    last = project(1, k, [0])
                last.then_inc(seg0_done, 1)
                turn(b, 0)
                for k in range(K):
                    project(1, k, [1])
                lora(b, 0)
                turn(b, 1)
                for k in range(K):
                    project(1, k, [2])
                lora(b, 1)

            pe.wait_ge(zeros_set, 1)
            for _ in range(WARM):
                nc.tensor.matmul(acc2[:, 0, 0, :], zeros[:, 0:P], zeros[:], start=True, stop=True)
            with pe.Fori(0, NB) as b:
                stage1(b)
                stage2(b)


def kernel(x, itok_B_1_14, itok_B_0_7, L0_cond_weight, L1_cond_W, L1_cond_Wr, L1_cond_A, L1_cond_B):
    import numpy as np
    import concourse.bacc as bacc
    from concourse.bass_utils import run_bass_kernel_spmd

    x, weight, W, Wr, A, B = (np.asarray(a) for a in (x, L0_cond_weight, L1_cond_W, L1_cond_Wr, L1_cond_A, L1_cond_B))
    n_adapters = weight.shape[0]
    xT = x.transpose(0, 2, 1).reshape(NB, K, P, TOK).transpose(0, 2, 1, 3)
    w_adapt = weight.reshape(n_adapters, OT, P, K, P).transpose(0, 1, 4, 3, 2).reshape(n_adapters, OT, P, K * P)
    WT = W.T
    cut = OUT_N[0]
    w_res = np.concatenate([WT[:, :cut], A.reshape(ER, D).T, Wr.T, WT[:, cut:]], axis=1).reshape(K, P, ROW)
    b_lora = B.transpose(0, 2, 1).reshape(ER, D)
    arrays = {
        "xT": xT,
        "adapter_ids": np.asarray(itok_B_1_14).reshape(1, NB),
        "lang_ids": np.broadcast_to(np.asarray(itok_B_0_7), (P, NB)),
        "w_adapt": w_adapt,
        "w_res": w_res,
        "b_lora": b_lora,
    }
    arrays = {name: np.ascontiguousarray(a) for name, a in arrays.items()}

    nc = bacc.Bacc("TRN2", target_bir_lowering=False, num_devices=1)
    aps = [nc.dram_tensor(name, a.shape, mybir.dt.from_np(a.dtype), kind="ExternalInput").ap()
           for name, a in arrays.items()]
    out = nc.dram_tensor("out", (NB, TOK, D), F32, kind="ExternalOutput").ap()
    build(nc, *aps, out)
    got = run_bass_kernel_spmd(nc, [arrays], core_ids=[0])
    return got.results[0]["out"]
```
